# Optimizing a Trainium2 kernel written in Bass

```python
import numpy as np
import jax
import jax.numpy as jnp

def _softmax(x, axis=-1):
    return jax.nn.softmax(x, axis=axis)

def _gelu(x):
    return jax.nn.gelu(x, approximate=True)

def _silu(x):
    return jax.nn.silu(x)

def _sigmoid(x):
    return jax.nn.sigmoid(x)

def _layernorm(x, axis=-1, eps=1e-05):
    m = jnp.mean(x, axis=axis, keepdims=True)
    v = jnp.var(x, axis=axis, keepdims=True)
    return (x - m) / jnp.sqrt(v + eps)

def _scatter_add(tgt, idx, src, axis=0):
    return tgt.at[idx].add(src)

def _segment_sum(src, seg, n):
    return jax.ops.segment_sum(src, seg, n)
kernel_name = 'mk_dlrm_tower_d1_rec_r8_61515e'

def setup_inputs(seed: int=0):
    np.random.seed(seed)
    _w = jnp.asarray

    def _rec_inputs():
        import jax
        import jax.numpy as jnp
        _tk = jax.random.key(seed)
        ids = jnp.stack([jax.random.randint(jax.random.fold_in(_tk, 200 + f), (512,), 0, v, jnp.int32) for f, v in enumerate([1000, 1250, 125000, 12500, 1250, 1250, 1250, 1250, 1250, 1000, 1250, 12500, 1000, 1250, 12500, 12500, 1000, 1000, 12500, 1000, 12500, 12500, 1000, 12500, 1250, 1000])], axis=1)
        tbl_0 = 0.05 * jax.random.normal(jax.random.fold_in(_tk, 500 + 0), (1000, 128), jnp.float32)
        tbl_1 = 0.05 * jax.random.normal(jax.random.fold_in(_tk, 500 + 1), (1250, 128), jnp.float32)
        tbl_2 = 0.05 * jax.random.normal(jax.random.fold_in(_tk, 500 + 2), (125000, 128), jnp.float32)
        tbl_3 = 0.05 * jax.random.normal(jax.random.fold_in(_tk, 500 + 3), (12500, 128), jnp.float32)
        tbl_4 = 0.05 * jax.random.normal(jax.random.fold_in(_tk, 500 + 4), (1250, 128), jnp.float32)
        tbl_5 = 0.05 * jax.random.normal(jax.random.fold_in(_tk, 500 + 5), (1250, 128), jnp.float32)
        tbl_6 = 0.05 * jax.random.normal(jax.random.fold_in(_tk, 500 + 6), (1250, 128), jnp.float32)
        tbl_7 = 0.05 * jax.random.normal(jax.random.fold_in(_tk, 500 + 7), (1250, 128), jnp.float32)
        tbl_8 = 0.05 * jax.random.normal(jax.random.fold_in(_tk, 500 + 8), (1250, 128), jnp.float32)
        tbl_9 = 0.05 * jax.random.normal(jax.random.fold_in(_tk, 500 + 9), (1000, 128), jnp.float32)
        tbl_10 = 0.05 * jax.random.normal(jax.random.fold_in(_tk, 500 + 10), (1250, 128), jnp.float32)
        tbl_11 = 0.05 * jax.random.normal(jax.random.fold_in(_tk, 500 + 11), (12500, 128), jnp.float32)
        tbl_12 = 0.05 * jax.random.normal(jax.random.fold_in(_tk, 500 + 12), (1000, 128), jnp.float32)
        tbl_13 = 0.05 * jax.random.normal(jax.random.fold_in(_tk, 500 + 13), (1250, 128), jnp.float32)
        tbl_14 = 0.05 * jax.random.normal(jax.random.fold_in(_tk, 500 + 14), (12500, 128), jnp.float32)
        tbl_15 = 0.05 * jax.random.normal(jax.random.fold_in(_tk, 500 + 15), (12500, 128), jnp.float32)
        tbl_16 = 0.05 * jax.random.normal(jax.random.fold_in(_tk, 500 + 16), (1000, 128), jnp.float32)
        tbl_17 = 0.05 * jax.random.normal(jax.random.fold_in(_tk, 500 + 17), (1000, 128), jnp.float32)
        tbl_18 = 0.05 * jax.random.normal(jax.random.fold_in(_tk, 500 + 18), (12500, 128), jnp.float32)
        tbl_19 = 0.05 * jax.random.normal(jax.random.fold_in(_tk, 500 + 19), (1000, 128), jnp.float32)
        tbl_20 = 0.05 * jax.random.normal(jax.random.fold_in(_tk, 500 + 20), (12500, 128), jnp.float32)
        tbl_21 = 0.05 * jax.random.normal(jax.random.fold_in(_tk, 500 + 21), (12500, 128), jnp.float32)
        tbl_22 = 0.05 * jax.random.normal(jax.random.fold_in(_tk, 500 + 22), (1000, 128), jnp.float32)
        tbl_23 = 0.05 * jax.random.normal(jax.random.fold_in(_tk, 500 + 23), (12500, 128), jnp.float32)
        tbl_24 = 0.05 * jax.random.normal(jax.random.fold_in(_tk, 500 + 24), (1250, 128), jnp.float32)
        tbl_25 = 0.05 * jax.random.normal(jax.random.fold_in(_tk, 500 + 25), (1000, 128), jnp.float32)
        _rk = jax.random.fold_in(_tk, 7)
        r_dense_proj = -0.000520686 + 1.00062 * jax.random.normal(jax.random.fold_in(_rk, 101), (512, 128), jnp.float32)
        W_top1 = 0.0405887 * jax.random.normal(jax.random.fold_in(_tk, 801), (607, 512), jnp.float32)
        W_top2 = 0.0441942 * jax.random.normal(jax.random.fold_in(_tk, 802), (512, 256), jnp.float32)
        W_top3 = 0.0625 * jax.random.normal(jax.random.fold_in(_tk, 803), (256, 1), jnp.float32)
        b_top1 = jnp.zeros((512,), jnp.float32)
        b_top2 = jnp.zeros((256,), jnp.float32)
        return (r_dense_proj, ids, tbl_0, tbl_1, tbl_2, tbl_3, tbl_4, tbl_5, tbl_6, tbl_7, tbl_8, tbl_9, tbl_10, tbl_11, tbl_12, tbl_13, tbl_14, tbl_15, tbl_16, tbl_17, tbl_18, tbl_19, tbl_20, tbl_21, tbl_22, tbl_23, tbl_24, tbl_25, W_top1, b_top1, W_top2, b_top2, W_top3)
    r_dense_proj, ids, tbl_0, tbl_1, tbl_2, tbl_3, tbl_4, tbl_5, tbl_6, tbl_7, tbl_8, tbl_9, tbl_10, tbl_11, tbl_12, tbl_13, tbl_14, tbl_15, tbl_16, tbl_17, tbl_18, tbl_19, tbl_20, tbl_21, tbl_22, tbl_23, tbl_24, tbl_25, W_top1, b_top1, W_top2, b_top2, W_top3 = _rec_inputs()

    def _L0_rec_setup():
        import jax, jax.numpy as jnp
        import numpy as np
        key = jax.random.key(seed)
        k1, k2 = jax.random.split(key)
        B, N_SPARSE, D = (2048, 26, 128)
        dense_proj = jax.random.normal(k1, (B, D), dtype=jnp.float32)
        sparse_embs = jax.random.normal(k2, (B, N_SPARSE, D), dtype=jnp.float32)
        return {'dense_proj': dense_proj, 'sparse_embs': sparse_embs}
    _L0_rec_all = _L0_rec_setup()
    _L0_rec_in = {k: v for k, v in _L0_rec_all.items() if k in ()}
    del _L0_rec_all
    return {'r_dense_proj': r_dense_proj, 'ids': ids, 'tbl_0': tbl_0, 'tbl_1': tbl_1, 'tbl_2': tbl_2, 'tbl_3': tbl_3, 'tbl_4': tbl_4, 'tbl_5': tbl_5, 'tbl_6': tbl_6, 'tbl_7': tbl_7, 'tbl_8': tbl_8, 'tbl_9': tbl_9, 'tbl_10': tbl_10, 'tbl_11': tbl_11, 'tbl_12': tbl_12, 'tbl_13': tbl_13, 'tbl_14': tbl_14, 'tbl_15': tbl_15, 'tbl_16': tbl_16, 'tbl_17': tbl_17, 'tbl_18': tbl_18, 'tbl_19': tbl_19, 'tbl_20': tbl_20, 'tbl_21': tbl_21, 'tbl_22': tbl_22, 'tbl_23': tbl_23, 'tbl_24': tbl_24, 'tbl_25': tbl_25, 'W_top1': W_top1, 'b_top1': b_top1, 'W_top2': W_top2, 'b_top2': b_top2, 'W_top3': W_top3}

def reference(r_dense_proj, ids, tbl_0, tbl_1, tbl_2, tbl_3, tbl_4, tbl_5, tbl_6, tbl_7, tbl_8, tbl_9, tbl_10, tbl_11, tbl_12, tbl_13, tbl_14, tbl_15, tbl_16, tbl_17, tbl_18, tbl_19, tbl_20, tbl_21, tbl_22, tbl_23, tbl_24, tbl_25, W_top1, b_top1, W_top2, b_top2, W_top3):
    import jax
    import jax.numpy as jnp

    def _L0_rec_ref(dense_proj, sparse_embs):
        import jax, jax.numpy as jnp
        import numpy as np
        all_vecs = jnp.concatenate([dense_proj[:, None, :], sparse_embs], axis=1)
        n = all_vecs.shape[1]
        interactions = jnp.einsum('bnd,bmd->bnm', all_vecs, all_vecs)
        rows, cols = np.triu_indices(n, k=1)
        interact_flat = interactions[:, rows, cols]
        return jnp.concatenate([dense_proj, interact_flat], axis=1)
    e = jnp.stack([tbl_0[ids[:, 0]], tbl_1[ids[:, 1]], tbl_2[ids[:, 2]], tbl_3[ids[:, 3]], tbl_4[ids[:, 4]], tbl_5[ids[:, 5]], tbl_6[ids[:, 6]], tbl_7[ids[:, 7]], tbl_8[ids[:, 8]], tbl_9[ids[:, 9]], tbl_10[ids[:, 10]], tbl_11[ids[:, 11]], tbl_12[ids[:, 12]], tbl_13[ids[:, 13]], tbl_14[ids[:, 14]], tbl_15[ids[:, 15]], tbl_16[ids[:, 16]], tbl_17[ids[:, 17]], tbl_18[ids[:, 18]], tbl_19[ids[:, 19]], tbl_20[ids[:, 20]], tbl_21[ids[:, 21]], tbl_22[ids[:, 22]], tbl_23[ids[:, 23]], tbl_24[ids[:, 24]], tbl_25[ids[:, 25]]], axis=1)
    z = _L0_rec_ref(r_dense_proj, e)
    z = z.reshape(z.shape[0], -1)
    h = jnp.concatenate([z, r_dense_proj], axis=1)
    h = jnp.maximum(h @ W_top1 + b_top1, 0.0)
    h = jnp.maximum(h @ W_top2 + b_top2, 0.0)
    y = h @ W_top3
    return y

_drawn_inputs = setup_inputs


def setup_inputs(seed=0):
    import zlib

    import numpy as np

    out = dict(_drawn_inputs(seed))
    spreads = {'b_top1': (0.0, 0.1), 'b_top2': (0.0, 0.1)}
    factors = {}
    for name, (base, spread) in spreads.items():
        noise = np.random.default_rng([zlib.crc32(name.encode()), seed]).standard_normal(out[name].shape)
        drawn = base * np.exp(spread * noise) if base else spread * noise
        out[name] = jnp.asarray(drawn.astype(out[name].dtype))
    for name, factor in factors.items():
        out[name] = (out[name] * factor).astype(out[name].dtype)
    return out
```

```python
import concourse.bass as bass
from concourse import mybir
from contextlib import ExitStack


def dlrm_tower(nc, dense, ids, tables, w1, b1, w2, b2, w3, y_out):
    fp32 = mybir.dt.float32
    ALU = mybir.AluOpType
    ACT = mybir.ActivationFunctionType

    P = 128
    B, D = dense.shape
    F = len(tables)
    NV = F + 1
    H1, H2 = w2.shape
    TILES = B // P
    OC1, OC2 = H1 // P, H2 // P

    SLOTS = 32
    UP = 16
    FIRST_UP = NV - UP

    def slot(v):
        return v - FIRST_UP if v >= FIRST_UP else UP + v

    UNITS = [[0]]
    v = F
    while v > 0:
        low = max(v - 3, FIRST_UP if v >= FIRST_UP else 1)
        UNITS.append(list(range(low, v + 1)))
        v = low - 1
    NU = len(UNITS)
    UP_UNITS = 1 + UP // 4
    assert NU % 2 == 0

    QUAD = P // SLOTS
    NQ = P // QUAD
    RQ = NQ // 2
    QCOLS = 1024 // RQ
    CU = UP // QUAD
    CL = 3
    NL = CL * QUAD
    CH = CU + CL
    DVE_SAMPLES, ACT_SAMPLES = (0, 1), (2, 3)

    def chunk(n):
        if n >= FIRST_UP:
            return (n - FIRST_UP) // CU, (n - FIRST_UP) % CU
        return n // CL, CU + n % CL

    def pair_row(n, m):
        return D + n * NV - n * (n + 1) // 2 + m - n - 1

    PAIRS = NV * (NV - 1) // 2
    ids_v = ids.rearrange("(t p) f -> t p f", p=P)
    dense_v = dense.rearrange("(t p) d -> t p d", p=P)

    ctx = ExitStack()
    with ctx:
        def sb(name, shape, dt=fp32):
            return ctx.enter_context(nc.sbuf_tensor(name, shape, dt))

        def pb(name, shape):
            return ctx.enter_context(nc.psum_tensor(name, shape, fp32))

        def sem(name):
            return ctx.enter_context(nc.semaphore(name))

        ident = sb("ident", [P, P])
        idx = sb("idx", [P, F], mybir.dt.int32)
        vecs = sb("vecs", [P, NV, D])
        xT = sb("xT", [P, P, SLOTS])
        denseT = sb("denseT", [P, P])
        gram = sb("gram", [P, CH, P])
        w1p = sb("w1p", [P, CH, H1])
        w1d = sb("w1d", [P, 2, H1])
        w2s = sb("w2s", [P, OC1, H2])
        w3s = sb("w3s", [P, OC2])
        b1s = sb("b1s", [P, OC1])
        b2s = sb("b2s", [P, OC2])
        h1 = sb("h1", [P, OC1, P])
        h2 = sb("h2", [P, OC2, P])
        y_row = sb("y_row", [1, B])

        ps_t = [pb(f"ps_t{i}", [P, 4, P]) for i in range(2)]
        ps_g = [pb(f"ps_g{i}", [P, RQ, QCOLS]) for i in range(2)]
        ps_m = [pb(f"ps_m{i}", [P, 4, P]) for i in range(2)]
        ps_y = ps_m[0][0:1, 1, :]

        zeroed = sem("zeroed")
        xT_zeroed = sem("xT_zeroed")
        ident_zero = sem("ident_zero")
        ident_ready = sem("ident_ready")
        idx_up = sem("idx_up")
        idx_low = sem("idx_low")
        dense_in = sem("dense_in")
        gathers_begun = sem("gathers_begun")
        gathered = [sem(f"gathered{k}") for k in range(NU)]
        w1d_in = sem("w1d_in")
        w1p_in = sem("w1p_in")
        w2_in = sem("w2_in")
        bias_in = sem("bias_in")
        transposed = sem("transposed")
        xT_dve = sem("xT_dve")
        xT_act = sem("xT_act")
        dots = [sem(f"dots{r}") for r in range(2)]
        gram_dve = [sem(f"gram_dve{r}") for r in range(2)]
        gram_act = [sem(f"gram_act{r}") for r in range(2)]
        h1_sums = sem("h1_sums")
        h1_dve = sem("h1_dve")
        h1_act = sem("h1_act")
        h2_sums = sem("h2_sums")
        h2_dve = sem("h2_dve")
        h2_act = sem("h2_act")
        y_sums = sem("y_sums")
        y_copied = sem("y_copied")
        y_stored = sem("y_stored")

        low_f = FIRST_UP - 1

        def load_idx_up(eng, t):
            eng.dma_start(idx[:, low_f:F], ids_v[t][:, low_f:F]).then_inc(idx_up, 16)

        def load_idx_low(eng, t):
            eng.dma_start(idx[:, 0:low_f], ids_v[t][:, 0:low_f]).then_inc(idx_low, 16)

        def load_dense(eng, t):
            eng.dma_start(vecs[:, 0, :], dense_v[t]).then_inc(dense_in, 16)

        def evacuate_unit(copy, k):
            vs = UNITS[k]
            s = slot(vs[0])
            src = ps_t[k % 2][:, 0:len(vs), :].rearrange("p v b -> p b v")
            return copy(xT[:, :, s:s + len(vs)], src)

        def evacuate_gram(copy, r, base, nch, samples):
            for s in samples:
                for g in range(QUAD):
                    src = ps_g[r][SLOTS * s:SLOTS * (s + 1), :, 0:QUAD * QUAD * nch]
                    src = src.rearrange("p q (s g c) -> p s g c q", s=QUAD, c=nch)[:, s, g]
                    dst = gram[SLOTS * g:SLOTS * (g + 1), base:base + nch, r * RQ * QUAD:(r + 1) * RQ * QUAD]
                    dst = dst.rearrange("p c (q s) -> p s c q", s=QUAD)[:, s]
                    last = copy(dst, src)
            return last

        def wait(eng, signal, value):
            if not isinstance(value, int) or value > 0:
                eng.wait_ge(signal, value)

        block = ctx.enter_context(nc.Block())

        @block.sync
        def _(sp):
            load_idx_up(sp, 0)
            load_dense(sp, 0)
            load_idx_low(sp, 0)
            sp.dma_start(w1d[:, 0, :], w1[0:D, :]).then_inc(w1d_in, 16)
            sp.dma_start(w1d[:, 1, :], w1[D + PAIRS:D + PAIRS + D, :]).then_inc(w1d_in, 16)
            sp.wait_ge(zeroed, 1)
            for n in range(F - 1, -1, -1):
                g, c = chunk(n)
                m = max(n + 1, FIRST_UP)
                p0 = SLOTS * g + slot(m)
                sp.dma_start(w1p[p0:p0 + NV - m, c, :],
                             w1[pair_row(n, m):pair_row(n, m) + NV - m, :]).then_inc(w1p_in, 16)
                if n + 1 < FIRST_UP:
                    p0 = SLOTS * g + slot(n + 1)
                    k = FIRST_UP - n - 1
                    sp.dma_start(w1p[p0:p0 + k, c, :],
                                 w1[pair_row(n, n + 1):pair_row(n, n + 1) + k, :]).then_inc(w1p_in, 16)
            with nc.allow_non_contiguous_dma(reason="biases and the last layer, once, under 2 KB each"):
                sp.dma_start(b1s[:, :], b1.rearrange("(c p) -> p c", p=P)).then_inc(bias_in, 16)
                sp.dma_start(b2s[:, :], b2.rearrange("(c p) -> p c", p=P)).then_inc(bias_in, 16)
                sp.dma_start(w2s[:, :, :], w2.rearrange("(c p) n -> p c n", p=P)).then_inc(w2_in, 16)
                sp.dma_start(w3s[:, :], w3.rearrange("(c p) o -> p (c o)", p=P)).then_inc(w2_in, 16)
            for t in range(1, TILES):
                sp.wait_ge(transposed, NU * (t - 1) + 1)
                load_dense(sp, t)
                sp.wait_ge(transposed, NU * (t - 1) + UP_UNITS)
                load_idx_up(sp, t)
                sp.wait_ge(transposed, NU * t)
                load_idx_low(sp, t)
            sp.wait_ge(y_copied, TILES)
            sp.dma_start(y_out.rearrange("b o -> o b"), y_row[:, :]).then_inc(y_stored, 16)
            sp.wait_ge(y_stored, 16)

        n_w1p = (F + FIRST_UP - 1) * 16

        @block.gpsimd
        def _(pool):
            nc.gpsimd.memset(ident[:], 0.0).then_inc(ident_zero, 1)
            pool.wait_ge(ident_zero, 1)
            nc.gpsimd.affine_select(out=ident[:], in_=ident[:], compare_op=ALU.not_equal, fill=1.0, base=0,
                                    pattern=[[-1, P]], channel_multiplier=1).then_inc(ident_ready, 1)

            def gather_tile(t):
                for k in range(1, NU):
                    if k == 1:
                        pool.wait_ge(idx_up, 16 * (t + 1))
                        pool.sem_inc(gathers_begun, 1)
                    if k == UP_UNITS:
                        pool.wait_ge(idx_low, 16 * (t + 1))
                        pool.sem_inc(gathers_begun, 1)
                    for v in reversed(UNITS[k]):
                        nc.gpsimd.indirect_dma_start(
                            vecs[:, v, :], None, tables[v - 1],
                            bass.IndirectOffsetOnAxis(ap=idx[:, v - 1:v].bitcast(mybir.dt.uint32), axis=0),
                        ).then_inc(gathered[k], 16)

            gather_tile(0)
            with pool.Fori(1, TILES) as t:
                gather_tile(t)

        @block.tensor
        def _(pe):
            xT_moved = [xT_dve, xT_act]

            def transpose_unit(t, k):
                if k == 0:
                    pe.wait_ge(dense_in, 16 * (t + 1))
                else:
                    pe.wait_ge(gathered[k], 16 * len(UNITS[k]) * (t + 1))
                wait(pe, xT_moved[k % 2], (NU // 2) * t + k // 2)
                for i, v in enumerate(UNITS[k]):
                    last = nc.tensor.matmul(ps_t[k % 2][:, i, :], vecs[:, v, :], ident[:], start=True, stop=True,
                                            is_transpose=True)
                last.then_inc(transposed, 1)

            def dot_products(t, upper):
                for r in range(2):
                    wait(pe, gram_dve[r], 2 * t + (0 if upper else 1))
                    wait(pe, gram_act[r], 2 * t + (0 if upper else 1))
                    for q in range(RQ):
                        b = (r * RQ + q) * QUAD
                        m = xT[:, b:b + QUAD, :].rearrange("p b s -> p (b s)")
                        n = xT[:, b:b + QUAD, 0:UP] if upper else xT[:, b:b + QUAD, UP:UP + NL]
                        out = ps_g[r][:, q, 0:QUAD * (UP if upper else NL)]
                        last = nc.tensor.matmul(out, m, n, start=True, stop=True)
                    last.then_inc(dots[r], 1)

            def h1_add(w, x, start=False, stop=False):
                for o in range(OC1):
                    last = nc.tensor.matmul(ps_m[o // 2][:, o % 2, :], w[:, o * P:(o + 1) * P], x,
                                            start=start and o % 2 == 0, stop=stop and o % 2 == 1,
                                            skip_group_check=True)
                return last

            pe.wait_ge(ident_ready, 1)

            def tile(t):
                for k in range(UP_UNITS):
                    transpose_unit(t, k)
                pe.wait_ge(xT_dve, (NU // 2) * t + (UP_UNITS + 1) // 2)
                pe.wait_ge(xT_act, (NU // 2) * t + UP_UNITS // 2)
                dot_products(t, True)
                pe.wait_ge(w1d_in, 32)
                wait(pe, y_copied, t)
                for i in range(2):
                    h1_add(w1d[:, i, :], denseT[:], start=(i == 0))
                transpose_unit(t, UP_UNITS)
                pe.wait_ge(w1p_in, n_w1p)
                for r in range(2):
                    pe.wait_ge(gram_dve[r], 2 * t + 1)
                    pe.wait_ge(gram_act[r], 2 * t + 1)
                for c in range(CU):
                    h1_add(w1p[:, c, :], gram[:, c, :])
                for k in range(UP_UNITS + 1, NU):
                    transpose_unit(t, k)
                pe.wait_ge(xT_dve, (NU // 2) * (t + 1))
                pe.wait_ge(xT_act, (NU // 2) * (t + 1))
                dot_products(t, False)
                for r in range(2):
                    pe.wait_ge(gram_dve[r], 2 * t + 2)
                    pe.wait_ge(gram_act[r], 2 * t + 2)
                for c in range(CU, CH):
                    last = h1_add(w1p[:, c, :], gram[:, c, :], stop=(c == CH - 1))
                last.then_inc(h1_sums, 1)
                pe.wait_ge(w2_in, 32)
                pe.wait_ge(h1_dve, t + 1)
                pe.wait_ge(h1_act, t + 1)
                for o in range(OC2):
                    for c in range(OC1):
                        last = nc.tensor.matmul(ps_m[o][:, 0, :], w2s[:, c, o * P:(o + 1) * P], h1[:, c, :],
                                                start=(c == 0), stop=(c == OC1 - 1))
                last.then_inc(h2_sums, 1)
                pe.wait_ge(h2_dve, t + 1)
                pe.wait_ge(h2_act, t + 1)
                for c in range(OC2):
                    last = nc.tensor.matmul(ps_y, w3s[:, c:c + 1], h2[:, c, :], start=(c == 0), stop=(c == OC2 - 1))
                last.then_inc(y_sums, 1)

            tile(0)
            with pe.Fori(1, TILES) as t:
                tile(t)

        @block.vector
        def _(dve):
            copy = nc.vector.tensor_copy
            nc.vector.memset(xT[:, :, UP + 1:SLOTS], 0.0).then_inc(xT_zeroed, 1)
            nc.vector.memset(w1p[:], 0.0).then_inc(zeroed, 1)

            def tile(t):
                for k in range(0, UP_UNITS, 2):
                    dve.wait_ge(transposed, NU * t + k + 1)
                    if k == 0:
                        copy(denseT[:], ps_t[0][:, 0, :])
                    evacuate_unit(copy, k).then_inc(xT_dve, 1)
                for r in range(2):
                    dve.wait_ge(dots[r], 2 * t + 1)
                    evacuate_gram(copy, r, 0, CU, DVE_SAMPLES).then_inc(gram_dve[r], 1)
                for k in range((UP_UNITS + 1) // 2 * 2, NU, 2):
                    dve.wait_ge(transposed, NU * t + k + 1)
                    evacuate_unit(copy, k).then_inc(xT_dve, 1)
                for r in range(2):
                    dve.wait_ge(dots[r], 2 * t + 2)
                    evacuate_gram(copy, r, CU, CL, DVE_SAMPLES).then_inc(gram_dve[r], 1)
                dve.wait_ge(bias_in, 32)
                dve.wait_ge(h1_sums, t + 1)
                for o in range(2):
                    last = nc.vector.tensor_scalar(h1[:, o, :], ps_m[0][:, o, :], b1s[:, o:o + 1], 0.0, ALU.add, ALU.max)
                last.then_inc(h1_dve, 1)
                dve.wait_ge(h2_sums, t + 1)
                nc.vector.tensor_scalar(h2[:, 0, :], ps_m[0][:, 0, :], b2s[:, 0:1], 0.0, ALU.add,
                                        ALU.max).then_inc(h2_dve, 1)
                dve.wait_ge(y_sums, t + 1)
                copy(y_row[:, bass.ts(t, P)], ps_y).then_inc(y_copied, 1)

            tile(0)
            with dve.Fori(1, TILES) as t:
                tile(t)

        @block.scalar
        def _(act):
            copy = nc.scalar.copy
            act.wait_ge(xT_zeroed, 1)

            def tile(t):
                for k in range(1, UP_UNITS, 2):
                    act.wait_ge(transposed, NU * t + k + 1)
                    evacuate_unit(copy, k).then_inc(xT_act, 1)
                for r in range(2):
                    act.wait_ge(dots[r], 2 * t + 1)
                    evacuate_gram(copy, r, 0, CU, ACT_SAMPLES).then_inc(gram_act[r], 1)
                for k in range(UP_UNITS // 2 * 2 + 1, NU, 2):
                    act.wait_ge(transposed, NU * t + k + 1)
                    evacuate_unit(copy, k).then_inc(xT_act, 1)
                for r in range(2):
                    act.wait_ge(dots[r], 2 * t + 2)
                    evacuate_gram(copy, r, CU, CL, ACT_SAMPLES).then_inc(gram_act[r], 1)
                act.wait_ge(bias_in, 32)
                act.wait_ge(h1_sums, t + 1)
                for o in range(2, OC1):
                    last = nc.scalar.activation(h1[:, o, :], ps_m[1][:, o - 2, :], ACT.Relu, bias=b1s[:, o:o + 1])
                last.then_inc(h1_act, 1)
                act.wait_ge(h2_sums, t + 1)
                nc.scalar.activation(h2[:, 1, :], ps_m[1][:, 0, :], ACT.Relu,
                                     bias=b2s[:, 1:2]).then_inc(h2_act, 1)

            tile(0)
            with act.Fori(1, TILES) as t:
                tile(t)


def kernel(**inputs):
    import numpy as np
    import concourse.bacc as bacc
    from concourse.bass_utils import run_bass_kernel_spmd

    nc = bacc.Bacc("TRN2", target_bir_lowering=False, num_devices=1)
    fields = inputs["ids"].shape[1]
    names = ["r_dense_proj", "ids"] + [f"tbl_{i}" for i in range(fields)]
    names += ["W_top1", "b_top1", "W_top2", "b_top2", "W_top3"]
    arrays, aps = {}, {}
    for name in names:
        a = np.ascontiguousarray(inputs[name])
        arrays[f"in_{name}"] = a
        aps[name] = nc.dram_tensor(f"in_{name}", a.shape, mybir.dt.from_np(a.dtype), kind="ExternalInput").ap()
    batch = inputs["ids"].shape[0]
    y = nc.dram_tensor("y", (batch, 1), mybir.dt.float32, kind="ExternalOutput").ap()
    dlrm_tower(nc, aps["r_dense_proj"], aps["ids"], [aps[f"tbl_{i}"] for i in range(fields)],
               aps["W_top1"], aps["b_top1"], aps["W_top2"], aps["b_top2"], aps["W_top3"], y)
    result = run_bass_kernel_spmd(nc, [arrays], core_ids=[0])
    return result.results[0]["y"]
```

```python
import concourse.bass as bass
from concourse import mybir
from contextlib import ExitStack


def dlrm_tower(nc, dense, ids, tables, w1, b1, w2, b2, w3, y_out):
    fp32 = mybir.dt.float32
    ALU = mybir.AluOpType
    ACT = mybir.ActivationFunctionType

    P = 128
    B, D = dense.shape
    F = len(tables)
    NV = F + 1
    H1, H2 = w2.shape
    TILES = B // P
    OC1, OC2 = H1 // P, H2 // P

    SLOTS = 32
    UP = 16
    FIRST_UP = NV - UP

    def slot(v):
        return v - FIRST_UP if v >= FIRST_UP else UP + v

    UNITS = [[0]]
    v = F
    while v > 0:
        low = max(v - 3, FIRST_UP if v >= FIRST_UP else 1)
        UNITS.append(list(range(low, v + 1)))
        v = low - 1
    NU = len(UNITS)
    UP_UNITS = 1 + UP // 4
    assert NU % 2 == 0

    QUAD = P // SLOTS
    NQ = P // QUAD
    SPAN = 1024
    CU = UP // QUAD
    CH = -(-NV // QUAD)
    ALL, UPPER, LOWER = (0, CH), (0, CU), (CU, CH)
    DVE_SAMPLES, ACT_SAMPLES = (0, 1), (2, 3)

    def chunk(n):
        return slot(n) % QUAD, slot(n) // QUAD

    def regions(part):
        quads = 4 if (part[1] - part[0]) * QUAD * QUAD > 64 else 8
        return NQ // (2 * quads), 2 * quads

    def pair_row(n, m):
        return D + n * NV - n * (n + 1) // 2 + m - n - 1

    PAIRS = NV * (NV - 1) // 2
    ids_v = ids.rearrange("(t p) f -> t p f", p=P)
    dense_v = dense.rearrange("(t p) d -> t p d", p=P)

    ctx = ExitStack()
    with ctx:
        def sb(name, shape, dt=fp32):
            return ctx.enter_context(nc.sbuf_tensor(name, shape, dt))

        def pb(name, shape):
            return ctx.enter_context(nc.psum_tensor(name, shape, fp32))

        def sem(name):
            return ctx.enter_context(nc.semaphore(name))

        ident = sb("ident", [P, P])
        idx = sb("idx", [P, F], mybir.dt.int32)
        vecs = sb("vecs", [P, NV, D])
        xT = sb("xT", [P, P, SLOTS])
        denseT = sb("denseT", [P, P])
        gram = sb("gram", [P, CH, P])
        w1p = sb("w1p", [P, CH, H1])
        w1d = sb("w1d", [P, 2, H1])
        w2s = sb("w2s", [P, OC1, H2])
        w3s = sb("w3s", [P, OC2])
        b1s = sb("b1s", [P, OC1])
        b2s = sb("b2s", [P, OC2])
        h1 = sb("h1", [P, OC1, P])
        h2 = sb("h2", [P, OC2, P])
        y_row = sb("y_row", [1, B])

        ps_t = [pb(f"ps_t{i}", [P, 4, P]) for i in range(2)]
        ps_g = [pb(f"ps_g{i}", [P, SPAN]) for i in range(2)]
        ps_h1 = [pb(f"ps_h1{i}", [P, 4, P]) for i in range(2)]
        ps_h2 = [ps_t[o][:, 0, :] for o in range(OC2)]
        ps_y = ps_h1[0][0:1, 0, :]

        zeroed = sem("zeroed")
        xT_zeroed = sem("xT_zeroed")
        ident_zero = sem("ident_zero")
        ident_ready = sem("ident_ready")
        idx_up = sem("idx_up")
        idx_low = sem("idx_low")
        dense_in = sem("dense_in")
        gathers_begun = sem("gathers_begun")
        gathered = [sem(f"gathered{k}") for k in range(NU)]
        w1d_in = sem("w1d_in")
        w1d_added = sem("w1d_added")
        w1p_in = sem("w1p_in")
        w2_in = sem("w2_in")
        bias_in = sem("bias_in")
        transposed = sem("transposed")
        xT_dve = sem("xT_dve")
        xT_act = sem("xT_act")
        dots = [sem(f"dots{r}") for r in range(2)]
        gram_dve = [sem(f"gram_dve{r}") for r in range(2)]
        gram_act = [sem(f"gram_act{r}") for r in range(2)]
        h1_sums = [sem(f"h1_sums{i}") for i in range(2)]
        h1_dve = sem("h1_dve")
        h1_act = sem("h1_act")
        h2_sums = sem("h2_sums")
        h2_dve = sem("h2_dve")
        h2_act = sem("h2_act")
        y_sums = sem("y_sums")
        y_copied = sem("y_copied")
        y_stored = sem("y_stored")

        low_f = FIRST_UP - 1

        def load_idx_up(eng, t):
            eng.dma_start(idx[:, low_f:F], ids_v[t][:, low_f:F]).then_inc(idx_up, 16)

        def load_idx_low(eng, t):
            eng.dma_start(idx[:, 0:low_f], ids_v[t][:, 0:low_f]).then_inc(idx_low, 16)

        def load_dense(eng, t):
            eng.dma_start(vecs[:, 0, :], dense_v[t]).then_inc(dense_in, 16)

        def evacuate_unit(copy, k):
            vs = UNITS[k]
            s = slot(vs[0])
            src = ps_t[k % 2][:, 0:len(vs), :].rearrange("p v b -> p b v")
            return copy(xT[:, :, s:s + len(vs)], src)

        def region_block(r, part, s):
            quads = regions(part)[1]
            nch = part[1] - part[0]
            block = ps_g[r][SLOTS * s:SLOTS * (s + 1), :].rearrange("p (q x) -> p q x", q=quads)
            block = block[:, :, 0:QUAD * QUAD * nch]
            return block.rearrange("p q (s c g) -> p s g c q", s=QUAD, g=QUAD)[:, s]

        def evacuate_gram(copy, i, part, samples):
            quads = regions(part)[1]
            for s in samples:
                for g in range(QUAD):
                    dst = gram[SLOTS * g:SLOTS * (g + 1), part[0]:part[1], i * quads * QUAD:(i + 1) * quads * QUAD]
                    dst = dst.rearrange("p c (q s) -> p s c q", s=QUAD)[:, s]
                    last = copy(dst, region_block(i % 2, part, s)[:, g])
            return last

        def wait(eng, signal, value):
            if not isinstance(value, int) or value > 0:
                eng.wait_ge(signal, value)

        block = ctx.enter_context(nc.Block())

        @block.sync
        def _(sp):
            load_idx_up(sp, 0)
            load_dense(sp, 0)
            load_idx_low(sp, 0)
            sp.dma_start(w1d[:, 0, :], w1[0:D, :]).then_inc(w1d_in, 16)
            sp.dma_start(w1d[:, 1, :], w1[D + PAIRS:D + PAIRS + D, :]).then_inc(w1d_in, 16)
            sp.wait_ge(zeroed, 1)
            for n in range(F - 1, -1, -1):
                g, c = chunk(n)
                m = max(n + 1, FIRST_UP)
                p0 = SLOTS * g + slot(m)
                sp.dma_start(w1p[p0:p0 + NV - m, c, :],
                             w1[pair_row(n, m):pair_row(n, m) + NV - m, :]).then_inc(w1p_in, 16)
                if n + 1 < FIRST_UP:
                    p0 = SLOTS * g + slot(n + 1)
                    k = FIRST_UP - n - 1
                    sp.dma_start(w1p[p0:p0 + k, c, :],
                                 w1[pair_row(n, n + 1):pair_row(n, n + 1) + k, :]).then_inc(w1p_in, 16)
            with nc.allow_non_contiguous_dma(reason="biases and the last layer, once, under 2 KB each"):
                sp.dma_start(b1s[:, :], b1.rearrange("(c p) -> p c", p=P)).then_inc(bias_in, 16)
                sp.dma_start(b2s[:, :], b2.rearrange("(c p) -> p c", p=P)).then_inc(bias_in, 16)
                sp.dma_start(w2s[:, :, :], w2.rearrange("(c p) n -> p c n", p=P)).then_inc(w2_in, 16)
                sp.dma_start(w3s[:, :], w3.rearrange("(c p) o -> p (c o)", p=P)).then_inc(w2_in, 16)
            for t in range(1, TILES):
                sp.wait_ge(transposed, NU * (t - 1) + 1)
                load_dense(sp, t)
                sp.wait_ge(transposed, NU * (t - 1) + UP_UNITS)
                load_idx_up(sp, t)
                sp.wait_ge(transposed, NU * t)
                load_idx_low(sp, t)
            sp.wait_ge(y_copied, TILES)
            sp.dma_start(y_out.rearrange("b o -> o b"), y_row[:, :]).then_inc(y_stored, 16)
            sp.wait_ge(y_stored, 16)

        n_w1p = (F + FIRST_UP - 1) * 16

        @block.gpsimd
        def _(pool):
            nc.gpsimd.memset(ident[:], 0.0).then_inc(ident_zero, 1)
            pool.wait_ge(ident_zero, 1)
            nc.gpsimd.affine_select(out=ident[:], in_=ident[:], compare_op=ALU.not_equal, fill=1.0, base=0,
                                    pattern=[[-1, P]], channel_multiplier=1).then_inc(ident_ready, 1)

            def gather_tile(t):
                for k in range(1, NU):
                    if k == 1:
                        pool.wait_ge(idx_up, 16 * (t + 1))
                        pool.sem_inc(gathers_begun, 1)
                    if k == UP_UNITS:
                        pool.wait_ge(idx_low, 16 * (t + 1))
                        pool.sem_inc(gathers_begun, 1)
                    for v in reversed(UNITS[k]):
                        nc.gpsimd.indirect_dma_start(
                            vecs[:, v, :], None, tables[v - 1],
                            bass.IndirectOffsetOnAxis(ap=idx[:, v - 1:v].bitcast(mybir.dt.uint32), axis=0),
                        ).then_inc(gathered[k], 16)

            gather_tile(0)
            with pool.Fori(1, TILES) as t:
                gather_tile(t)

        @block.tensor
        def _(pe):
            xT_moved = [xT_dve, xT_act]

            def transpose_unit(t, k):
                if k == 0:
                    pe.wait_ge(dense_in, 16 * (t + 1))
                else:
                    pe.wait_ge(gathered[k], 16 * len(UNITS[k]) * (t + 1))
                wait(pe, xT_moved[k % 2], (NU // 2) * t + k // 2)
                for i, v in enumerate(UNITS[k]):
                    last = nc.tensor.matmul(ps_t[k % 2][:, i, :], vecs[:, v, :], ident[:], start=True, stop=True,
                                            is_transpose=True)
                last.then_inc(transposed, 1)

            def dot_products(t, part):
                fills, quads = regions(part)
                for i in range(fills):
                    before = 2 * t + i // 2 + (1 if part is LOWER else 0)
                    wait(pe, gram_dve[i % 2], before)
                    wait(pe, gram_act[i % 2], before)
                    for q in range(quads):
                        b = (i * quads + q) * QUAD
                        m = xT[:, b:b + QUAD, :].rearrange("p b s -> p (b s)")
                        n = xT[:, b:b + QUAD, part[0] * QUAD:part[1] * QUAD]
                        at = q * (SPAN // quads)
                        out = ps_g[i % 2][:, at:at + QUAD * QUAD * (part[1] - part[0])]
                        last = nc.tensor.matmul(out, m, n, start=True, stop=True)
                    last.then_inc(dots[i % 2], 1)

            def h1_add(w, x, start=False):
                for o in range(OC1):
                    nc.tensor.matmul(ps_h1[o // 2][:, o % 2, :], w[:, o * P:(o + 1) * P], x,
                                     start=start and o % 2 == 0, stop=False, skip_group_check=True)

            def h1_add_chunks(part, start):
                for c in range(*part):
                    h1_add(w1p[:, c, :], gram[:, c, :], start and c == part[0])

            def h1_add_last(c):
                for o in range(OC1):
                    last = nc.tensor.matmul(ps_h1[o // 2][:, o % 2, :], w1p[:, c, o * P:(o + 1) * P], gram[:, c, :],
                                            start=False, stop=o % 2 == 1, skip_group_check=True)
                    if o % 2 == 1:
                        last.then_inc(h1_sums[o // 2], 1)

            def wait_xT(t, units):
                pe.wait_ge(xT_dve, (NU // 2) * t + (units + 1) // 2)
                pe.wait_ge(xT_act, (NU // 2) * t + units // 2)

            def wait_gram(count):
                for r in range(2):
                    pe.wait_ge(gram_dve[r], count)
                    pe.wait_ge(gram_act[r], count)

            def upper_layers(t):
                pe.wait_ge(w2_in, 32)
                for c in range(OC1):
                    if c == 0:
                        pe.wait_ge(h1_dve, t + 1)
                    if c == 2:
                        pe.wait_ge(h1_act, t + 1)
                    for o in range(OC2):
                        last = nc.tensor.matmul(ps_h2[o], w2s[:, c, o * P:(o + 1) * P], h1[:, c, :],
                                                start=(c == 0), stop=(c == OC1 - 1))
                last.then_inc(h2_sums, 1)
                for c in range(OC2):
                    pe.wait_ge(h2_dve if c == 0 else h2_act, t + 1)
                    last = nc.tensor.matmul(ps_y, w3s[:, c:c + 1], h2[:, c, :], start=(c == 0), stop=(c == OC2 - 1))
                last.then_inc(y_sums, 1)

            def tile(t):
                for k in range(NU):
                    transpose_unit(t, k)
                wait_xT(t, NU)
                dot_products(t, ALL)
                pe.wait_ge(w1d_added, 1)
                wait(pe, y_copied, t)
                h1_add(w1d[:, 0, :], denseT[:], start=True)
                pe.wait_ge(w1p_in, n_w1p)
                wait_gram(2 * t + 2)
                h1_add_chunks((0, CH - 1), start=False)
                h1_add_last(CH - 1)
                upper_layers(t)

            def last_tile(t):
                for k in range(UP_UNITS):
                    transpose_unit(t, k)
                wait_xT(t, UP_UNITS)
                dot_products(t, UPPER)
                transpose_unit(t, UP_UNITS)
                wait_gram(2 * t + 1)
                pe.wait_ge(y_copied, t)
                h1_add_chunks(UPPER, start=True)
                for k in range(UP_UNITS + 1, NU):
                    transpose_unit(t, k)
                wait_xT(t, NU)
                dot_products(t, LOWER)
                h1_add(w1d[:, 0, :], denseT[:])
                wait_gram(2 * t + 2)
                h1_add_chunks((CU, CH - 1), start=False)
                h1_add_last(CH - 1)
                upper_layers(t)

            pe.wait_ge(ident_ready, 1)
            tile(0)
            with pe.Fori(1, TILES - 1) as t:
                tile(t)
            last_tile(TILES - 1)

        @block.vector
        def _(dve):
            copy = nc.vector.tensor_copy
            nc.vector.memset(xT[:, :, UP + 1:SLOTS], 0.0).then_inc(xT_zeroed, 1)
            nc.vector.memset(w1p[:], 0.0).then_inc(zeroed, 1)

            def move_units(t, first, end):
                for k in range(first, end):
                    if k % 2 == 0:
                        dve.wait_ge(transposed, NU * t + k + 1)
                        if k == 0:
                            copy(denseT[:], ps_t[0][:, 0, :])
                        evacuate_unit(copy, k).then_inc(xT_dve, 1)

            def move_gram(t, part):
                for i in range(regions(part)[0]):
                    r = i % 2
                    dve.wait_ge(dots[r], 2 * t + i // 2 + (2 if part is LOWER else 1))
                    evacuate_gram(copy, i, part, DVE_SAMPLES).then_inc(gram_dve[r], 1)

            def layers(t):
                dve.wait_ge(h1_sums[0], t + 1)
                for o in range(2):
                    last = nc.vector.tensor_scalar(h1[:, o, :], ps_h1[0][:, o, :], b1s[:, o:o + 1], 0.0, ALU.add, ALU.max)
                last.then_inc(h1_dve, 1)
                dve.wait_ge(h2_sums, t + 1)
                nc.vector.tensor_scalar(h2[:, 0, :], ps_h2[0], b2s[:, 0:1], 0.0, ALU.add, ALU.max).then_inc(h2_dve, 1)
                dve.wait_ge(y_sums, t + 1)
                copy(y_row[:, bass.ts(t, P)], ps_y).then_inc(y_copied, 1)

            def tile(t):
                move_units(t, 0, NU)
                move_gram(t, ALL)
                layers(t)

            dve.wait_ge(w1d_in, 32)
            nc.vector.tensor_tensor(w1d[:, 0, :], w1d[:, 0, :], w1d[:, 1, :], ALU.add).then_inc(w1d_added, 1)
            move_units(0, 0, NU)
            move_gram(0, ALL)
            dve.wait_ge(bias_in, 32)
            layers(0)
            with dve.Fori(1, TILES - 1) as t:
                tile(t)
            move_units(TILES - 1, 0, UP_UNITS)
            move_gram(TILES - 1, UPPER)
            move_units(TILES - 1, UP_UNITS, NU)
            move_gram(TILES - 1, LOWER)
            layers(TILES - 1)

        @block.scalar
        def _(act):
            copy = nc.scalar.copy

            def move_units(t, first, end):
                for k in range(first, end):
                    if k % 2 == 1:
                        act.wait_ge(transposed, NU * t + k + 1)
                        evacuate_unit(copy, k).then_inc(xT_act, 1)

            def move_gram(t, part):
                for i in range(regions(part)[0]):
                    r = i % 2
                    act.wait_ge(dots[r], 2 * t + i // 2 + (2 if part is LOWER else 1))
                    evacuate_gram(copy, i, part, ACT_SAMPLES).then_inc(gram_act[r], 1)

            def layers(t):
                act.wait_ge(h1_sums[1], t + 1)
                for o in range(2):
                    last = nc.scalar.activation(h1[:, 2 + o, :], ps_h1[1][:, o, :], ACT.Relu, bias=b1s[:, 2 + o:3 + o])
                last.then_inc(h1_act, 1)
                act.wait_ge(h2_sums, t + 1)
                nc.scalar.activation(h2[:, 1, :], ps_h2[1], ACT.Relu, bias=b2s[:, 1:2]).then_inc(h2_act, 1)

            def tile(t):
                move_units(t, 0, NU)
                move_gram(t, ALL)
                layers(t)

            act.wait_ge(xT_zeroed, 1)
            move_units(0, 0, NU)
            move_gram(0, ALL)
            act.wait_ge(bias_in, 32)
            layers(0)
            with act.Fori(1, TILES - 1) as t:
                tile(t)
            move_units(TILES - 1, 0, UP_UNITS)
            move_gram(TILES - 1, UPPER)
            move_units(TILES - 1, UP_UNITS, NU)
            move_gram(TILES - 1, LOWER)
            layers(TILES - 1)


def kernel(**inputs):
    import numpy as np
    import concourse.bacc as bacc
    from concourse.bass_utils import run_bass_kernel_spmd

    nc = bacc.Bacc("TRN2", target_bir_lowering=False, num_devices=1)
    fields = inputs["ids"].shape[1]
    names = ["r_dense_proj", "ids"] + [f"tbl_{i}" for i in range(fields)]
    names += ["W_top1", "b_top1", "W_top2", "b_top2", "W_top3"]
    arrays, aps = {}, {}
    for name in names:
        a = np.ascontiguousarray(inputs[name])
        arrays[f"in_{name}"] = a
        aps[name] = nc.dram_tensor(f"in_{name}", a.shape, mybir.dt.from_np(a.dtype), kind="ExternalInput").ap()
    batch = inputs["ids"].shape[0]
    y = nc.dram_tensor("y", (batch, 1), mybir.dt.float32, kind="ExternalOutput").ap()
    dlrm_tower(nc, aps["r_dense_proj"], aps["ids"], [aps[f"tbl_{i}"] for i in range(fields)],
               aps["W_top1"], aps["b_top1"], aps["W_top2"], aps["b_top2"], aps["W_top3"], y)
    result = run_bass_kernel_spmd(nc, [arrays], core_ids=[0])
    return result.results[0]["y"]
```

```python
import concourse.bass as bass
from concourse import mybir
from contextlib import ExitStack


def dlrm_tower(nc, dense, ids, ids_t, tables, w1, b1, w2, b2, w3, y_out):
    fp32 = mybir.dt.float32
    bf16 = mybir.dt.bfloat16
    int32 = mybir.dt.int32
    ALU = mybir.AluOpType
    ACT = mybir.ActivationFunctionType

    P = 128
    B, D = dense.shape
    F = len(tables)
    NV = F + 1
    H1, H2 = w2.shape
    TILES = B // P
    OC1, OC2 = H1 // P, H2 // P
    PAIRS = NV * (NV - 1) // 2

    HOT_RUNS = [range(17, 27, 3), range(18, 19)]
    HOT = [v for run in HOT_RUNS for v in run]
    ROWS = tables[HOT[0] - 1].shape[0]
    PC = 8
    RP = ROWS // PC
    HI = PC // 2
    assert all(tables[v - 1].shape[0] == ROWS for v in HOT) and RP * PC == ROWS and RP <= P and ROWS < 2 ** 15

    ORDER = [v for v in range(F, -1, -1) if v not in HOT]
    UNITS = [ORDER[i:i + 4] for i in range(0, len(ORDER), 4)]
    NU = len(UNITS)
    PAIR_UNITS = 2
    UNITS_AFTER = [[], [0], [1, 2], [3, 4], [5]]
    assert NU == 6 and NU % PAIR_UNITS == 0 and len(HOT) == len(UNITS_AFTER)
    assert F - 1 in UNITS[0] and F in HOT_RUNS[0] and len(HOT_RUNS) == 2 and len(HOT_RUNS[1]) == 1

    def gathers_of(k):
        return 16 * len([v for v in UNITS[k] if v > 0])

    def pair_columns(i):
        vs = [v for k in range(PAIR_UNITS * i, PAIR_UNITS * (i + 1)) for v in UNITS[k] if v > 0]
        return slice(min(vs) - 1, max(vs))

    SLOTS = 32
    COPIES = 2
    QUAD = P // SLOTS
    CH = NV // QUAD
    COLS = NV - 1
    LEFT_OVER = range(CH * QUAD, COLS)
    assert len(LEFT_OVER) == COPIES
    SPAN = 128
    RQ = 1024 // SPAN
    FILLS = P // QUAD // RQ
    FILLED = FILLS // 2
    DVE_SAMPLES, ACT_SAMPLES = (0, 1), (2, 3)

    def pair_row(n, m):
        return D + n * NV - n * (n + 1) // 2 + m - n - 1

    ids_v = ids.rearrange("(t p) f -> t p f", p=P)
    dense_v = dense.rearrange("(t p) d -> t p d", p=P)

    ctx = ExitStack()
    with ctx:
        def sb(name, shape, dt=fp32):
            return ctx.enter_context(nc.sbuf_tensor(name, shape, dt))

        def pb(name, shape):
            return ctx.enter_context(nc.psum_tensor(name, shape, fp32))

        def sem(name):
            return ctx.enter_context(nc.semaphore(name))

        ident = sb("ident", [P, P])
        idx = sb("idx", [P, F], int32)
        vecs = sb("vecs", [P, NV, D])
        xT = sb("xT", [P, P, SLOTS])
        denseT = sb("denseT", [P, P])
        gram = sb("gram", [P, CH, P])
        w1p = sb("w1p", [P, CH, H1])
        w1d = sb("w1d", [P, 2, H1])
        w2s = sb("w2s", [P, OC1, H2])
        w3s = sb("w3s", [P, OC2])
        b1s = sb("b1s", [P, OC1])
        b2s = sb("b2s", [P, OC2])
        h1 = sb("h1", [P, OC1, P])
        h2 = sb("h2", [P, OC2, P])
        y_row = sb("y_row", [1, B])
        hot_ids = sb("hot_ids", [P, len(HOT), B], int32)
        hot_ids16 = sb("hot_ids16", [P, len(HOT), B], mybir.dt.int16)
        hot_table = sb("hot_table", [RP, len(HOT), PC, D])
        row_int = sb("row_int", [P, PC], int32)
        row_no = sb("row_no", [P, PC])
        hot_part = sb("hot_part", [RP, len(HOT), 3, PC, D], bf16)
        hot_left = sb("hot_left", [RP, 2, PC, D])
        one_hot = sb("one_hot", [RP, len(HOT), PC, B], bf16)
        zero = sb("zero", [P, 1])
        hotT = sb("hotT", [P, B, len(HOT)])

        ps_t = [pb(f"ps_t{i}", [P, 4, P]) for i in range(2)]
        ps_g = [pb(f"ps_g{i}", [P, RQ, SPAN]) for i in range(2)]
        ps_m = [pb(f"ps_m{i}", [P, 4, P]) for i in range(2)]
        ps_h1 = [ps_m[o // 2][:, o % 2, :] for o in range(OC1)]
        ps_h2 = [ps_g[o][:, 0, :] for o in range(OC2)]
        ps_y = ps_m[0][0:1, 2, :]
        ps_hot = [bank.rearrange("p a b -> p (a b)") for bank in
                  (ps_g[0][:, 0:4, :], ps_g[0][:, 4:8, :], ps_g[1][:, 0:4, :], ps_g[1][:, 4:8, :], ps_m[0][:, :, :])]

        w1p_zeroed = sem("w1p_zeroed")
        xT_zeroed = sem("xT_zeroed")
        ident_zero = sem("ident_zero")
        ident_ready = sem("ident_ready")
        rows_counted = sem("rows_counted")
        row_no_ready = sem("row_no_ready")
        hot_ids16_ready = sem("hot_ids16_ready")
        idx_in = [sem(f"idx_in{i}") for i in range(NU // PAIR_UNITS)]
        dense_in = sem("dense_in")
        gathers_begun = sem("gathers_begun")
        gathered = [sem(f"gathered{k}") for k in range(NU)]
        hot_ids_in = [sem(f"hot_ids_in{j}") for j in range(len(HOT))]
        hot_table_in = [sem(f"hot_table_in{j}") for j in range(len(HOT))]
        part_hi = sem("part_hi")
        part_left = sem("part_left")
        part_mid = sem("part_mid")
        part_lo = sem("part_lo")
        zero_ready = sem("zero_ready")
        one_hot_ready = sem("one_hot_ready")
        hot_sums = sem("hot_sums")
        hot_moved = sem("hot_moved")
        hot_placed = sem("hot_placed")
        copies_placed = sem("copies_placed")
        w1d_in = sem("w1d_in")
        w1d_added = sem("w1d_added")
        denseT_ready = sem("denseT_ready")
        w1p_in = sem("w1p_in")
        w2_in = sem("w2_in")
        bias_in = sem("bias_in")
        transposed = sem("transposed")
        xT_dve = sem("xT_dve")
        xT_act = sem("xT_act")
        dots = [sem(f"dots{r}") for r in range(2)]
        gram_dve = [sem(f"gram_dve{r}") for r in range(2)]
        gram_act = [sem(f"gram_act{r}") for r in range(2)]
        over_dve = [sem(f"over_dve{r}") for r in range(2)]
        over_act = [sem(f"over_act{r}") for r in range(2)]
        h1_sums = [sem(f"h1_sums{i}") for i in range(2)]
        h1_dve = sem("h1_dve")
        h1_act = sem("h1_act")
        h2_sums = [sem(f"h2_sums{o}") for o in range(2)]
        h2_dve = sem("h2_dve")
        h2_act = sem("h2_act")
        y_sums = sem("y_sums")
        y_copied = sem("y_copied")
        y_stored = sem("y_stored")

        def evacuate_unit(copy, k):
            vs = UNITS[k]
            a = 0
            while a < len(vs):
                e = a + 1
                while e < len(vs) and vs[e] == vs[e - 1] - 1:
                    e += 1
                lo = len(vs) - e
                src = ps_t[k % 2][:, lo:lo + e - a, :].rearrange("p v b -> p b v")
                last = copy(xT[:, :, COPIES + vs[e - 1]:COPIES + vs[a] + 1], src)
                a = e
            return last

        def evacuate_gram(copy, i, samples):
            for s in samples:
                own = ps_g[i % 2][SLOTS * s:SLOTS * (s + 1), :, s * COLS:s * COLS + QUAD * CH]
                own = own.rearrange("p q (c g) -> p g c q", g=QUAD)
                for g in range(QUAD):
                    dst = gram[SLOTS * g:SLOTS * (g + 1), :, i * RQ * QUAD:(i + 1) * RQ * QUAD]
                    dst = dst.rearrange("p c (q s) -> p s c q", s=QUAD)[:, s]
                    last = copy(dst, own[:, g])
            return last

        def evacuate_over(copy, i, samples):
            for s in samples:
                for g, n in enumerate(LEFT_OVER):
                    dst = gram[SLOTS * g:SLOTS * g + COPIES, CH - 1, i * RQ * QUAD:(i + 1) * RQ * QUAD]
                    dst = dst.rearrange("p (q s) -> p s q", s=QUAD)[:, s]
                    last = copy(dst, ps_g[i % 2][SLOTS * s:SLOTS * s + COPIES, :, s * COLS + n])
            return last

        def wait(eng, signal, value):
            if not isinstance(value, int) or value > 0:
                eng.wait_ge(signal, value)

        block = ctx.enter_context(nc.Block())

        @block.sync
        def _(sp):
            def load_idx(t, i):
                cols = pair_columns(i)
                sp.dma_start(idx[:, cols], ids_v[t][:, cols]).then_inc(idx_in[i], 16)

            def load_dense(t):
                sp.dma_start(vecs[:, 0, :], dense_v[t]).then_inc(dense_in, 16)

            load_idx(0, 0)
            for j, v in enumerate(HOT):
                sp.dma_start(hot_ids[:, j, :], ids_t[v - 1:v, :].to_broadcast([P, B])).then_inc(hot_ids_in[j], 16)
                sp.dma_start(hot_table[:, j, :, :], tables[v - 1].rearrange("(p c) d -> p c d", c=PC)
                             ).then_inc(hot_table_in[j], 16)
                if j == 0:
                    for i in range(1, NU // PAIR_UNITS):
                        load_idx(0, i)
            load_dense(0)
            sp.dma_start(w1d[:, 0, :], w1[0:D, :]).then_inc(w1d_in, 16)
            sp.dma_start(w1d[:, 1, :], w1[D + PAIRS:D + PAIRS + D, :]).then_inc(w1d_in, 16)
            with nc.allow_non_contiguous_dma(reason="biases and the last layer, once, under 2 KB each"):
                sp.dma_start(b1s[:, :], b1.rearrange("(c p) -> p c", p=P)).then_inc(bias_in, 16)
                sp.dma_start(b2s[:, :], b2.rearrange("(c p) -> p c", p=P)).then_inc(bias_in, 16)
                sp.dma_start(w2s[:, :, :], w2.rearrange("(c p) n -> p c n", p=P)).then_inc(w2_in, 16)
                sp.dma_start(w3s[:, :], w3.rearrange("(c p) o -> p (c o)", p=P)).then_inc(w2_in, 16)
            sp.wait_ge(w1p_zeroed, 1)
            for n in range(COLS):
                c, slot = (CH - 1, n - LEFT_OVER[0]) if n in LEFT_OVER else (n // QUAD, COPIES + n + 1)
                p0 = SLOTS * (n % QUAD) + slot
                sp.dma_start(w1p[p0:p0 + F - n, c, :],
                             w1[pair_row(n, n + 1):pair_row(n, F) + 1, :]).then_inc(w1p_in, 16)
            for t in range(1, TILES):
                for i in range(NU // PAIR_UNITS):
                    for k in range(PAIR_UNITS * i, PAIR_UNITS * (i + 1)):
                        sp.wait_ge(gathered[k], gathers_of(k) * t)
                    load_idx(t, i)
                sp.wait_ge(transposed, NU * t)
                load_dense(t)
            sp.wait_ge(y_copied, TILES)
            sp.dma_start(y_out.rearrange("b o -> o b"), y_row[:, :]).then_inc(y_stored, 16)
            sp.wait_ge(y_stored, 16)

        @block.gpsimd
        def _(pool):
            nc.gpsimd.memset(ident[:], 0.0).then_inc(ident_zero, 1)
            nc.gpsimd.iota(row_int[:], pattern=[[1, PC]], base=0, channel_multiplier=PC).then_inc(rows_counted, 1)
            pool.wait_ge(ident_zero, 1)
            nc.gpsimd.affine_select(out=ident[:], in_=ident[:], compare_op=ALU.not_equal, fill=1.0, base=0,
                                    pattern=[[-1, P]], channel_multiplier=1).then_inc(ident_ready, 1)

            def gather_unit(t, k):
                pool.wait_ge(idx_in[k // PAIR_UNITS], 16 * (t + 1))
                pool.sem_inc(gathers_begun, 1)
                for v in UNITS[k]:
                    if v > 0:
                        nc.gpsimd.indirect_dma_start(
                            vecs[:, v, :], None, tables[v - 1],
                            bass.IndirectOffsetOnAxis(ap=idx[:, v - 1:v].bitcast(mybir.dt.uint32), axis=0),
                        ).then_inc(gathered[k], 16)

            for k in range(NU):
                gather_unit(0, k)
            with pool.Fori(1, TILES) as t:
                for k in range(NU):
                    pool.wait_ge(transposed, NU * (t - 1) + k + 1)
                    gather_unit(t, k)

        @block.tensor
        def _(pe):
            xT_moved = [xT_dve, xT_act]

            def look_up(j):
                for i, part_ready in enumerate((part_hi, part_mid, part_lo)):
                    for c in range(PC):
                        if i == 0:
                            pe.wait_ge(one_hot_ready, PC * j + c + 1)
                            if c % HI == 0:
                                pe.wait_ge(part_hi, (PC * j + c) // HI + 1)
                        elif c == 0:
                            pe.wait_ge(part_ready, j + 1)
                        last = nc.tensor.matmul(ps_hot[j], hot_part[:, j, i, c, :], one_hot[:, j, c, :],
                                                start=(i == 0 and c == 0), stop=(i == 2 and c == PC - 1))
                last.then_inc(hot_sums, 1)

            def transpose_unit(t, k):
                pe.wait_ge(gathered[k], gathers_of(k) * (t + 1))
                if 0 in UNITS[k]:
                    pe.wait_ge(dense_in, 16 * (t + 1))
                wait(pe, xT_moved[k % 2], (NU // 2) * t + k // 2)
                for i, v in enumerate(reversed(UNITS[k])):
                    last = nc.tensor.matmul(ps_t[k % 2][:, i, :], vecs[:, v, :], ident[:], start=True, stop=True,
                                            is_transpose=True)
                last.then_inc(transposed, 1)

            def dot_products(t):
                pe.wait_ge(xT_dve, (NU // 2) * (t + 1))
                pe.wait_ge(xT_act, (NU // 2) * (t + 1))
                pe.wait_ge(hot_placed, len(HOT_RUNS) * (t + 1))
                pe.wait_ge(copies_placed, t + 1)
                for i in range(FILLS):
                    wait(pe, over_dve[i % 2], FILLED * t + i // 2)
                    wait(pe, over_act[i % 2], FILLED * t + i // 2)
                    for q in range(RQ):
                        b = (i * RQ + q) * QUAD
                        m = xT[:, b:b + QUAD, :].rearrange("p b s -> p (b s)")
                        n = xT[:, b:b + QUAD, COPIES:COPIES + COLS]
                        last = nc.tensor.matmul(ps_g[i % 2][:, q, 0:QUAD * COLS], m, n, start=True, stop=True)
                    last.then_inc(dots[i % 2], 1)

            def h1_add(w, x, start=False, stop=False):
                for o in range(OC1):
                    last = nc.tensor.matmul(ps_h1[o], w[:, o * P:(o + 1) * P], x, start=start and o % 2 == 0,
                                            stop=stop and o % 2 == 1, skip_group_check=True)
                    if stop and o % 2 == 1:
                        last.then_inc(h1_sums[o // 2], 1)

            def layer1(t, then_next):
                pe.wait_ge(w1d_added, 1)
                pe.wait_ge(hot_moved, len(HOT))
                wait(pe, y_copied, t)
                pe.wait_ge(denseT_ready, t + 1)
                h1_add(w1d[:, 0, :], denseT[:], start=True)
                pe.wait_ge(w1p_in, 16 * COLS)
                for r in range(2):
                    pe.wait_ge(gram_dve[r], FILLED * (t + 1))
                    pe.wait_ge(gram_act[r], FILLED * (t + 1))
                for c in range(CH):
                    if then_next and c == CH - 2:
                        transpose_unit(t + 1, 2)
                        transpose_unit(t + 1, 3)
                    if c == CH - 1:
                        for r in range(2):
                            pe.wait_ge(over_dve[r], FILLED * (t + 1))
                            pe.wait_ge(over_act[r], FILLED * (t + 1))
                    h1_add(w1p[:, c, :], gram[:, c, :], stop=(c == CH - 1))

            def layer2(t):
                pe.wait_ge(w2_in, 32)
                for c in range(OC1):
                    pe.wait_ge(h1_dve if c < 2 else h1_act, 2 * t + c % 2 + 1)
                    if c < 3:
                        for o in range(OC2):
                            nc.tensor.matmul(ps_h2[o], w2s[:, c, o * P:(o + 1) * P], h1[:, c, :],
                                             start=(c == 0), stop=False)
                    else:
                        for o in range(OC2):
                            nc.tensor.matmul(ps_h2[o], w2s[:, c, o * P:(o + 1) * P], h1[:, c, :], start=False,
                                             stop=True).then_inc(h2_sums[o], 1)

            def layer3(t):
                for c in range(OC2):
                    pe.wait_ge(h2_dve if c == 0 else h2_act, t + 1)
                    last = nc.tensor.matmul(ps_y, w3s[:, c:c + 1], h2[:, c, :], start=(c == 0), stop=(c == OC2 - 1))
                last.then_inc(y_sums, 1)

            def tile(t, then_next):
                dot_products(t)
                if then_next:
                    transpose_unit(t + 1, 0)
                    transpose_unit(t + 1, 1)
                layer1(t, then_next)
                layer2(t)
                if then_next:
                    transpose_unit(t + 1, 4)
                    transpose_unit(t + 1, 5)
                layer3(t)

            pe.wait_ge(ident_ready, 1)
            for j in range(len(HOT)):
                look_up(j)
                for k in UNITS_AFTER[j]:
                    transpose_unit(0, k)
            tile(0, True)
            with pe.Fori(1, TILES - 1) as t:
                tile(t, True)
            tile(TILES - 1, False)

        @block.vector
        def _(dve):
            copy = nc.vector.tensor_copy

            def build_one_hot(j):
                dve.wait_ge(hot_ids_in[j], 16)
                copy(hot_ids16[:, j, :], hot_ids[:, j, :]).then_inc(hot_ids16_ready, 1)
                dve.wait_ge(hot_ids16_ready, j + 1)
                for c in range(PC):
                    nc.vector.tensor_scalar(one_hot[:, j, c, :], hot_ids16[0:RP, j, :], row_no[0:RP, c:c + 1],
                                            None, ALU.is_equal).then_inc(one_hot_ready, 1)

            def take_hi(j):
                dve.wait_ge(part_hi, PC // HI * (j + 1))
                nc.vector.tensor_tensor(hot_left[:, j % 2], hot_table[:, j], hot_part[:, j, 0],
                                        ALU.subtract).then_inc(part_left, 1)

            def take_mid(j):
                dve.wait_ge(part_mid, j + 1)
                nc.vector.tensor_tensor(hot_part[:, j, 2], hot_left[:, j % 2], hot_part[:, j, 1],
                                        ALU.subtract).then_inc(part_lo, 1)

            def move_units(t, first, end):
                for k in range(first, end):
                    if k % 2 == 0:
                        dve.wait_ge(transposed, NU * t + k + 1)
                        evacuate_unit(copy, k).then_inc(xT_dve, 1)

            def move_gram(t):
                for i in range(FILLS):
                    dve.wait_ge(dots[i % 2], FILLED * t + i // 2 + 1)
                    evacuate_gram(copy, i, DVE_SAMPLES).then_inc(gram_dve[i % 2], 1)
                    dve.wait_ge(gram_dve[i % 2], FILLED * t + i // 2 + 1)
                    evacuate_over(copy, i, DVE_SAMPLES).then_inc(over_dve[i % 2], 1)

            def tile(t, then_next):
                move_gram(t)
                if then_next:
                    move_units(t + 1, 0, 4)
                dve.wait_ge(h1_sums[0], t + 1)
                for o in range(2):
                    nc.vector.tensor_scalar(h1[:, o, :], ps_h1[o], b1s[:, o:o + 1], 0.0, ALU.add,
                                            ALU.max).then_inc(h1_dve, 1)
                dve.wait_ge(h2_sums[0], t + 1)
                nc.vector.tensor_scalar(h2[:, 0, :], ps_h2[0], b2s[:, 0:1], 0.0, ALU.add, ALU.max).then_inc(h2_dve, 1)
                if then_next:
                    move_units(t + 1, 4, NU)
                dve.wait_ge(y_sums, t + 1)
                copy(y_row[:, bass.ts(t, P)], ps_y).then_inc(y_copied, 1)

            nc.vector.memset(zero[:], 0.0).then_inc(zero_ready, 1)
            nc.vector.memset(xT[:, :, COPIES + NV:SLOTS], 0.0).then_inc(xT_zeroed, 1)
            dve.wait_ge(rows_counted, 1)
            copy(row_no[:], row_int[:]).then_inc(row_no_ready, 1)
            dve.wait_ge(row_no_ready, 1)
            build_one_hot(0)
            take_hi(0)
            for j in range(len(HOT)):
                if j + 1 < len(HOT):
                    build_one_hot(j + 1)
                take_mid(j)
                if j + 1 < len(HOT):
                    take_hi(j + 1)
                if j > 0:
                    for k in UNITS_AFTER[j - 1]:
                        move_units(0, k, k + 1)
            for k in UNITS_AFTER[-1]:
                move_units(0, k, k + 1)
            dve.wait_ge(w1d_in, 32)
            nc.vector.tensor_tensor(w1d[:, 0, :], w1d[:, 0, :], w1d[:, 1, :], ALU.add).then_inc(w1d_added, 1)
            dve.wait_ge(bias_in, 32)
            tile(0, True)
            with dve.Fori(1, TILES - 1) as t:
                tile(t, True)
            tile(TILES - 1, False)

        @block.scalar
        def _(act):
            copy = nc.scalar.copy

            def place_run(t, r):
                run = HOT_RUNS[r]
                j = HOT.index(run[0])
                copy(xT[:, :, COPIES + run[0]:COPIES + run[-1] + 1:run.step],
                     hotT[:, bass.ts(t, P), j:j + len(run)]).then_inc(hot_placed, 1)

            def place_copies(t):
                act.wait_ge(xT_dve, (NU // 2) * t + 1)
                act.wait_ge(hot_placed, len(HOT_RUNS) * t + 1)
                copy(xT[:, :, 0:COPIES], xT[:, :, NV:NV + COPIES]).then_inc(copies_placed, 1)

            def place_hot(t):
                place_run(t, 0)
                place_copies(t)
                place_run(t, 1)

            def move_units(t, first, end):
                for k in range(first, end):
                    if k % 2 == 1:
                        act.wait_ge(transposed, NU * t + k + 1)
                        evacuate_unit(copy, k).then_inc(xT_act, 1)
                        if k == NU - 1:
                            copy(denseT[:], ps_t[k % 2][:, 0, :]).then_inc(denseT_ready, 1)

            def move_gram(t):
                for i in range(FILLS):
                    act.wait_ge(dots[i % 2], FILLED * t + i // 2 + 1)
                    evacuate_gram(copy, i, ACT_SAMPLES).then_inc(gram_act[i % 2], 1)
                    act.wait_ge(gram_act[i % 2], FILLED * t + i // 2 + 1)
                    evacuate_over(copy, i, ACT_SAMPLES).then_inc(over_act[i % 2], 1)

            def tile(t, then_next):
                move_gram(t)
                if then_next:
                    move_units(t + 1, 0, 2)
                    place_hot(t + 1)
                    move_units(t + 1, 2, 4)
                act.wait_ge(h1_sums[1], t + 1)
                for o in range(2, OC1):
                    nc.scalar.activation(h1[:, o, :], ps_h1[o], ACT.Relu, bias=b1s[:, o:o + 1]).then_inc(h1_act, 1)
                act.wait_ge(h2_sums[1], t + 1)
                nc.scalar.activation(h2[:, 1, :], ps_h2[1], ACT.Relu, bias=b2s[:, 1:2]).then_inc(h2_act, 1)
                if then_next:
                    move_units(t + 1, 4, NU)

            def round_hi(j):
                act.wait_ge(hot_table_in[j], 16)
                for c in range(0, PC, HI):
                    copy(hot_part[:, j, 0, c:c + HI], hot_table[:, j, c:c + HI]).then_inc(part_hi, 1)

            def round_mid(j):
                act.wait_ge(part_left, j + 1)
                copy(hot_part[:, j, 1], hot_left[:, j % 2]).then_inc(part_mid, 1)

            act.wait_ge(zero_ready, 1)
            copy(w1p[:], zero[:].unsqueeze(2).to_broadcast([P, CH, H1])).then_inc(w1p_zeroed, 1)
            round_hi(0)
            round_mid(0)
            round_hi(1)
            act.wait_ge(xT_zeroed, 1)
            for j, v in enumerate(HOT):
                if j + 1 < len(HOT):
                    round_mid(j + 1)
                if j + 2 < len(HOT):
                    round_hi(j + 2)
                act.wait_ge(hot_sums, j + 1)
                if j == len(HOT) - 1:
                    copy(xT[:, :, COPIES + v], ps_hot[j][:, 0:P]).then_inc(hot_placed, 1)
                for k in UNITS_AFTER[j]:
                    move_units(0, k, k + 1)
                copy(hotT[:, :, j], ps_hot[j]).then_inc(hot_moved, 1)
                if v == HOT_RUNS[0][-1]:
                    act.wait_ge(hot_moved, j + 1)
                    place_run(0, 0)
                    place_copies(0)
            act.wait_ge(hot_moved, len(HOT))
            act.wait_ge(bias_in, 32)
            tile(0, True)
            with act.Fori(1, TILES - 1) as t:
                tile(t, True)
            tile(TILES - 1, False)


def kernel(**inputs):
    import numpy as np
    import concourse.bacc as bacc
    from concourse.bass_utils import run_bass_kernel_spmd

    nc = bacc.Bacc("TRN2", target_bir_lowering=False, num_devices=1)
    fields = inputs["ids"].shape[1]
    names = ["r_dense_proj", "ids"] + [f"tbl_{i}" for i in range(fields)]
    names += ["W_top1", "b_top1", "W_top2", "b_top2", "W_top3"]
    arrays, aps = {}, {}
    for name in names:
        a = np.ascontiguousarray(inputs[name])
        arrays[f"in_{name}"] = a
        aps[name] = nc.dram_tensor(f"in_{name}", a.shape, mybir.dt.from_np(a.dtype), kind="ExternalInput").ap()
    arrays["in_ids_t"] = np.ascontiguousarray(np.asarray(inputs["ids"]).T)
    ids_t = nc.dram_tensor("in_ids_t", arrays["in_ids_t"].shape, mybir.dt.from_np(arrays["in_ids_t"].dtype),
                           kind="ExternalInput").ap()
    batch = inputs["ids"].shape[0]
    y = nc.dram_tensor("y", (batch, 1), mybir.dt.float32, kind="ExternalOutput").ap()
    dlrm_tower(nc, aps["r_dense_proj"], aps["ids"], ids_t, [aps[f"tbl_{i}"] for i in range(fields)],
               aps["W_top1"], aps["b_top1"], aps["W_top2"], aps["b_top2"], aps["W_top3"], y)
    result = run_bass_kernel_spmd(nc, [arrays], core_ids=[0])
    return result.results[0]["y"]
```
